# Optimizing a Trainium2 kernel written in Bass

```python
import numpy as np
import jax
import jax.numpy as jnp

def _softmax(x, axis=-1):
    return jax.nn.softmax(x, axis=axis)

def _gelu(x):
    return jax.nn.gelu(x, approximate=True)

def _silu(x):
    return jax.nn.silu(x)

def _sigmoid(x):
    return jax.nn.sigmoid(x)

def _layernorm(x, axis=-1, eps=1e-05):
    m = jnp.mean(x, axis=axis, keepdims=True)
    v = jnp.var(x, axis=axis, keepdims=True)
    return (x - m) / jnp.sqrt(v + eps)

def _scatter_add(tgt, idx, src, axis=0):
    return tgt.at[idx].add(src)

def _segment_sum(src, seg, n):
    return jax.ops.segment_sum(src, seg, n)
kernel_name = 'mk_rec_standalone_d1_rec_r8_07ea0b'

def setup_inputs(seed: int=0):
    np.random.seed(seed)
    _w = jnp.asarray

    def _rec_inputs():
        import jax
        import jax.numpy as jnp
        _rk = jax.random.key(seed)
        r_inputs = jax.random.uniform(jax.random.fold_in(_rk, 1), (1024, 12500), jnp.float32, 0.0, 1)
        return r_inputs
    r_inputs = _rec_inputs()

    def _L0_rec_setup():
        import jax, jax.numpy as jnp
        import numpy as np
        BATCH = 256
        BUCKETS = 12500
        DIM = 64
        key = jax.random.key(seed)
        k1, k2 = jax.random.split(key)
        inputs = jax.random.uniform(k1, (BATCH, BUCKETS), dtype=jnp.float32)
        embeddings = jax.random.normal(k2, (BUCKETS, DIM), dtype=jnp.float32)
        return {'inputs': inputs, 'embeddings': embeddings}
    _L0_rec_all = _L0_rec_setup()
    _L0_rec_in = {k: v for k, v in _L0_rec_all.items() if k in ('embeddings',)}
    del _L0_rec_all
    return {'r_inputs': r_inputs, 'L0_rec_embeddings': _L0_rec_in['embeddings']}

def reference(r_inputs, L0_rec_embeddings):
    import jax
    import jax.numpy as jnp

    def _L0_rec_ref(inputs, embeddings):
        import jax, jax.numpy as jnp
        import numpy as np
        BATCH = 256
        BUCKETS = 12500
        DIM = 64
        out = jnp.matmul(inputs, embeddings)
        s = jnp.sum(inputs, axis=-1, keepdims=True)
        out = jnp.where(s > 0, out / s, jnp.zeros_like(out))
        return out
    y = _L0_rec_ref(r_inputs, L0_rec_embeddings)
    return y

_drawn_inputs = setup_inputs


def setup_inputs(seed=0):
    import zlib

    import numpy as np

    out = dict(_drawn_inputs(seed))
    spreads = {}
    factors = {}
    for name, (base, spread) in spreads.items():
        noise = np.random.default_rng([zlib.crc32(name.encode()), seed]).standard_normal(out[name].shape)
        drawn = base * np.exp(spread * noise) if base else spread * noise
        out[name] = jnp.asarray(drawn.astype(out[name].dtype))
    for name, factor in factors.items():
        out[name] = (out[name] * factor).astype(out[name].dtype)
    return out
```

```python
import concourse.bass as bass
from concourse import mybir
from contextlib import ExitStack



def rec_kernel(nc: bass.Bass, x: bass.AP, emb: bass.AP, out: bass.AP):
    fp32 = mybir.dt.float32
    bf16 = mybir.dt.bfloat16
    u32 = mybir.dt.uint32
    ALU = mybir.AluOpType
    ACT = mybir.ActivationFunctionType
    AX = mybir.AxisListType

    BATCH, BUCKETS = x.shape
    DIM = emb.shape[1]
    P = 128
    ROWS = 32
    QUARTERS = P // ROWS
    QCOLS = BUCKETS // QUARTERS
    PAIR = 2 * ROWS
    PAIRS = 7
    CHUNKS = 2 * PAIRS
    COLS = PAIRS * PAIR
    STEPS = -(-QCOLS // COLS)
    LAST = STEPS - 1
    LAST_COLS = QCOLS - LAST * COLS
    LAST_FULL = LAST_COLS // PAIR
    LAST_REST = LAST_COLS % PAIR
    TILES = 4
    GROUPS = BATCH // ROWS // TILES
    TROWS = GROUPS * ROWS
    LOOPED = 6
    assert LOOPED == LAST and LOOPED % 2 == 0 and QCOLS * QUARTERS == BUCKETS

    x_view = x.rearrange("(g r) (i k) -> i r g k", r=ROWS, i=QUARTERS)

    def emb_rows(i, start, pairs):
        a = i * QCOLS + start
        return emb[bass.ds(a, pairs * PAIR), :].rearrange("(q r t) d -> r q (t d)", r=ROWS, t=2)

    ctx = ExitStack()
    with ctx:
        def sb(name, shape, dt=fp32):
            return ctx.enter_context(nc.sbuf_tensor(name, shape, dt))

        def ps(name):
            return ctx.enter_context(nc.psum_tensor(name, [P, 512], fp32))

        def sem(name):
            return ctx.enter_context(nc.semaphore(name))

        xt = [sb(f"x_tile{k}", [P, GROUPS, COLS]) for k in range(TILES)]
        tt = [sb(f"transposed{k}", [P, CHUNKS, TROWS]) for k in range(TILES)]
        et = [sb(f"emb{n}", [P, PAIRS, 2 * DIM]) for n in range(2)]
        e_last = sb("emb_last", [P, PAIRS, 2 * DIM])
        dump = sb("dump", [P, GROUPS, COLS], bf16)
        partial = sb("partial_sums", [P, STEPS, TILES * GROUPS])
        quarter_sums = sb("quarter_sums", [P, TILES * GROUPS])
        ident = sb("ident", [P, P])
        fold = sb("fold", [P, ROWS])
        zeros = sb("zeros", [P, TROWS], bf16)
        acc_sb = [sb(f"acc_sb{h}", [P, TROWS]) for h in range(2)]
        rowsum = sb("rowsum", [P, TILES * 2])
        inverse = sb("inverse", [P, TILES * 2])
        positive = sb("positive", [P, TILES * 2], u32)
        scaled = sb("scaled", [P, 4, 2, DIM])
        result = sb("result", [P, 4, 2, DIM])

        acc = [ps(f"acc{h}") for h in range(2)]
        sum_ps = ps("sum_ps")
        flip = ps("flip")

        x_landed = [sem(f"x_landed{k}") for k in range(TILES)]
        e_landed = [sem(f"e_landed{n}") for n in range(2)]
        e_last_landed = sem("e_last_landed")
        tile_transposed = sem("tile_transposed")
        tile_summed = sem("tile_summed")
        half_multiplied = [sem(f"half_multiplied{h}") for h in range(2)]
        zeros_ready = sem("zeros_ready")
        pads_ready = sem("pads_ready")
        pad_cleared = sem("pad_cleared")
        ident_zeroed = sem("ident_zeroed")
        ident_ready = sem("ident_ready")
        fold_ready = sem("fold_ready")
        quarters_ready = sem("quarters_ready")
        sums_folded = sem("sums_folded")
        scale_ready = sem("scale_ready")
        acc_copied = sem("acc_copied")
        flipped = sem("flipped")
        vec = sem("vec")
        result_ready = sem("result_ready")
        stored = sem("stored")

        block = ctx.enter_context(nc.Block())

        def held(eng, value):
            return value if isinstance(value, int) else eng.snap(value)

        def load_x(eng, quarters, k, start, cols=COLS):
            for i in quarters:
                eng.dma_start(xt[k][ROWS * i:ROWS * (i + 1), :, 0:cols],
                              x_view[i, :, GROUPS * k:GROUPS * (k + 1), bass.ds(start, cols)]
                              ).then_inc(x_landed[k], 16)

        def load_e(eng, quarters, n, start):
            for i in quarters:
                eng.dma_start(et[n][ROWS * i:ROWS * (i + 1), :, :],
                              emb_rows(i, start, PAIRS)).then_inc(e_landed[n], 16)

        def load_e_last(eng, quarters):
            eng.wait_ge(pads_ready, 1)
            for i in quarters:
                p = ROWS * i
                start = LAST * COLS
                eng.dma_start(e_last[p:p + ROWS, 0:LAST_FULL, :],
                              emb_rows(i, start, LAST_FULL)).then_inc(e_last_landed, 16)
                row = i * QCOLS + start + LAST_FULL * PAIR
                both = LAST_REST // 2
                eng.dma_start(e_last[p:p + both, LAST_FULL, :],
                              emb[row:row + 2 * both, :].rearrange("(r t) d -> r (t d)", t=2)
                              ).then_inc(e_last_landed, 16)
                if LAST_REST % 2:
                    eng.dma_start(e_last[p + both:p + both + 1, LAST_FULL, 0:DIM],
                                  emb[row + 2 * both:row + 2 * both + 1, :]).then_inc(e_last_landed, 16)
        E_LAST = 16 * QUARTERS * (2 + LAST_REST % 2)

        def first_loads(eng, quarters):
            load_e(eng, quarters, 0, 0)
            for k in range(TILES):
                load_x(eng, quarters, k, 0)
            load_e(eng, quarters, 1, COLS)

        @block.sync
        def _(sp):
            mine = (1, 0)

            def refill(s, cols=COLS):
                start = held(sp, (s + 1) * COLS)
                for k in range(TILES):
                    done = held(sp, 4 * s + k + 1)
                    sp.wait_ge(tile_transposed, done)
                    sp.wait_ge(tile_summed, done)
                    load_x(sp, mine, k, start, cols)

            first_loads(sp, mine)
            with sp.Fori(0, LOOPED // 2 - 1, 1) as two:
                for n in range(2):
                    refill(two * 2 + n)
                    done = held(sp, two * 2 + (n + 2))
                    start = held(sp, two * (2 * COLS) + (n + 2) * COLS)
                    sp.wait_ge(half_multiplied[1], done)
                    load_e(sp, mine, n, start)
            load_e_last(sp, mine)
            refill(LAST - 2)
            refill(LAST - 1, LAST_COLS)
            sp.wait_ge(result_ready, 1)
            out_view = out.rearrange("(h a u p) d -> p h u a d", h=2, a=2, u=2)
            for h in range(2):
                for u in range(2):
                    sp.dma_start(out_view[:, h, u, :, :], result[:, 2 * h + u, :, :]).then_inc(stored, 16)
            sp.wait_ge(stored, 64)

        @block.scalar
        def _(act):
            mine = (2, 3)

            def sum_tile(s, k, cols=COLS):
                act.wait_ge(x_landed[k], 64 * (s + 1))
                for n in range(GROUPS):
                    last = nc.scalar.activation(dump[:, n, 0:cols], xt[k][:, n, 0:cols], ACT.Copy,
                                                accum_out=partial[:, bass.ds(s, 1), GROUPS * k + n])
                last.then_inc(tile_summed, 1)

            def sum_and_refill(s, cols=COLS):
                start = held(act, (s + 1) * COLS)
                for k in range(TILES):
                    done = held(act, 4 * s + k + 1)
                    sum_tile(s, k)
                    act.wait_ge(tile_summed, done)
                    act.wait_ge(tile_transposed, done)
                    load_x(act, mine, k, start, cols)

            first_loads(act, mine)
            with act.Fori(0, LOOPED // 2 - 1, 1) as two:
                for n in range(2):
                    sum_and_refill(two * 2 + n)
                    done = held(act, two * 2 + (n + 2))
                    start = held(act, (two * 2 + (n + 2)) * COLS)
                    act.wait_ge(half_multiplied[1], done)
                    load_e(act, mine, n, start)
            load_e_last(act, mine)
            sum_and_refill(LAST - 2)
            sum_and_refill(LAST - 1, LAST_COLS)
            for k in range(TILES):
                act.wait_ge(tile_summed, 4 * LAST + k)
                sum_tile(LAST, k, LAST_COLS)

        @block.gpsimd
        def _(pool):
            nc.gpsimd.memset(zeros[:], 0.0).then_inc(zeros_ready, 1)
            nc.gpsimd.memset(e_last[:, LAST_FULL, :], 0.0).then_inc(pads_ready, 1)
            nc.gpsimd.memset(ident[:], 0.0).then_inc(ident_zeroed, 1)
            pool.wait_ge(ident_zeroed, 1)
            nc.gpsimd.affine_select(out=ident[:], in_=ident[:], compare_op=ALU.not_equal, fill=1.0, base=0,
                                    pattern=[[-1, P]], channel_multiplier=1).then_inc(ident_ready, 1)

        @block.vector
        def _(dve):
            def transpose_tile(s, k):
                dve.wait_ge(x_landed[k], 64 * (s + 1))
                if k % 2 == 0:
                    dve.wait_ge(half_multiplied[k // 2], s + 1)
                if isinstance(s, int) and s == LAST:
                    nc.vector.memset(xt[k][:, :, LAST_COLS:COLS], 0.0).then_inc(pad_cleared, 1)
                    dve.wait_ge(pad_cleared, k + 1)
                for n in range(GROUPS):
                    last = nc.vector.transpose(
                        tt[k][:, :, ROWS * n:ROWS * (n + 1)].rearrange("p (q t) c -> p q t c", t=2),
                        xt[k][:, n, :].rearrange("p (q r t) -> p q t r", t=2, r=ROWS))
                last.then_inc(tile_transposed, 1)

            dve.wait_ge(ident_ready, 1)
            nc.vector.tensor_reduce(fold[:], ident[:].rearrange("p (i r) -> p r i", r=ROWS),
                                    AX.X, ALU.add).then_inc(fold_ready, 1)
            with dve.Fori(0, LOOPED, 1) as s:
                for k in range(TILES):
                    transpose_tile(s, k)
            for k in range(TILES):
                transpose_tile(LAST, k)
            dve.wait_ge(tile_summed, TILES * STEPS)
            nc.vector.tensor_reduce(quarter_sums[:], partial[:].rearrange("p s g -> p g s"),
                                    AX.X, ALU.add).then_inc(quarters_ready, 1)
            dve.wait_ge(sums_folded, 1)
            nc.vector.tensor_copy(rowsum[:], sum_ps[:, 0:8]).then_inc(vec, 1)
            nc.vector.memset(result[:], 0.0)
            dve.wait_ge(vec, 1)
            nc.vector.tensor_scalar(positive[:], rowsum[:], 0.0, None, ALU.is_gt).then_inc(scale_ready, 1)
            nc.vector.reciprocal(inverse[:], rowsum[:]).then_inc(scale_ready, 1)
            for h in range(2):
                dve.wait_ge(half_multiplied[h], STEPS + 1)
                nc.vector.tensor_copy(acc_sb[h][:], acc[h][:, 0:TROWS]).then_inc(acc_copied, 1)
            dve.wait_ge(flipped, 1)
            dve.wait_ge(scale_ready, 2)

            def per_block(t):
                return t[:].rearrange("p (h a u) -> p h u a", h=2, a=2)

            for h in range(2):
                nc.vector.tensor_tensor(
                    scaled[:, 2 * h:2 * h + 2, :, :],
                    flip[:, 2 * P * h:2 * P * (h + 1)].rearrange("p (u a d) -> p u a d", u=2, a=2),
                    per_block(inverse)[:, h, :, :].unsqueeze(3).broadcast_to((P, 2, 2, DIM)),
                    ALU.mult).then_inc(vec, 1)
            dve.wait_ge(vec, 3)
            for h in range(2):
                last = nc.vector.copy_predicated(
                    result[:, 2 * h:2 * h + 2, :, :],
                    per_block(positive)[:, h, :, :].unsqueeze(3).broadcast_to((P, 2, 2, DIM)),
                    scaled[:, 2 * h:2 * h + 2, :, :])
            last.then_inc(result_ready, 1)

        @block.tensor
        def _(pe):
            def multiply(s, h, e, last=False):
                pe.wait_ge(tile_transposed, 4 * s + 2 * h + 2)
                for j in range(CHUNKS):
                    for a in range(2):
                        mm = nc.tensor.matmul(acc[h][64 * a:64 * a + 64, 0:TROWS],
                                              e[:, j // 2, DIM * (j % 2):DIM * (j % 2 + 1)],
                                              tt[2 * h + a][:, j, :],
                                              start=False, stop=last and j == CHUNKS - 1)
                mm.then_inc(half_multiplied[h], 1)

            pe.wait_ge(zeros_ready, 1)
            for h in range(2):
                for a in range(2):
                    mm = nc.tensor.matmul(acc[h][64 * a:64 * a + 64, 0:TROWS], zeros[:, 0:DIM], zeros[:],
                                          start=True, stop=False)
                mm.then_inc(half_multiplied[h], 1)
            with pe.Fori(0, LOOPED // 2, 1) as two:
                for n in range(2):
                    pe.wait_ge(e_landed[n], 64 * two + 64)
                    for h in range(2):
                        multiply(two * 2 + n, h, et[n])
            pe.wait_ge(e_last_landed, E_LAST)
            for h in range(2):
                multiply(LAST, h, e_last, last=True)
            pe.wait_ge(fold_ready, 1)
            pe.wait_ge(quarters_ready, 1)
            by_part = quarter_sums[:].rearrange("p (b w) -> p w b", w=4)
            for w in range(4):
                mm = nc.tensor.matmul(sum_ps[ROWS * w:ROWS * (w + 1), 0:8], fold[:], by_part[:, w, :],
                                      start=True, stop=True)
            mm.then_inc(sums_folded, 1)
            for h in range(2):
                pe.wait_ge(acc_copied, h + 1)
                for u in range(2):
                    mm = nc.tensor.transpose(flip[:, P * (2 * h + u):P * (2 * h + u + 1)],
                                             acc_sb[h][:, P * u:P * (u + 1)], ident[:])
            mm.then_inc(flipped, 1)


_INS = ["r_inputs", "L0_rec_embeddings"]
_OUTS = [((1024, 64), "float32")]


def kernel(**inputs):
    import numpy as _np
    import concourse.bacc as _bacc
    from concourse import mybir as _mybir
    from concourse.bass_utils import run_bass_kernel_spmd as _run

    nc = _bacc.Bacc("TRN2", target_bir_lowering=False, num_devices=1)
    arrays, args = {}, []
    for name in _INS:
        a = _np.ascontiguousarray(inputs[name])
        arrays[f"in_{name}_dram"] = a
        args.append(nc.dram_tensor(f"in_{name}_dram", a.shape, _mybir.dt.from_np(a.dtype), kind="ExternalInput").ap())
    for i, (shape, dtype) in enumerate(_OUTS):
        dt = _mybir.dt.from_np(_np.dtype(dtype))
        args.append(nc.dram_tensor(f"out_{i}_dram", shape, dt, kind="ExternalOutput").ap())
    rec_kernel(nc, *args)
    r = _run(nc, [arrays], core_ids=[0])
    got = tuple(r.results[0][f"out_{i}_dram"] for i in range(len(_OUTS)))
    return got[0]
```

```python
import concourse.bass as bass
from concourse import mybir
from contextlib import ExitStack



def rec_kernel(nc: bass.Bass, x: bass.AP, emb: bass.AP, out: bass.AP):
    fp32 = mybir.dt.float32
    bf16 = mybir.dt.bfloat16
    u32 = mybir.dt.uint32
    ALU = mybir.AluOpType
    ACT = mybir.ActivationFunctionType
    AX = mybir.AxisListType

    BATCH, BUCKETS = x.shape
    DIM = emb.shape[1]
    P = 128
    ROWS = 32
    QUARTERS = P // ROWS
    QCOLS = BUCKETS // QUARTERS
    PAIR = 2 * ROWS
    PAIRS = 7
    CHUNKS = 2 * PAIRS
    COLS = PAIRS * PAIR
    STEPS = -(-QCOLS // COLS)
    LAST = STEPS - 1
    LAST_COLS = QCOLS - LAST * COLS
    LAST_FULL = LAST_COLS // PAIR
    LAST_REST = LAST_COLS % PAIR
    TILES = 4
    GROUPS = BATCH // ROWS // TILES
    TROWS = GROUPS * ROWS
    LOOPED = 6
    SPLIT = 4
    PARTS = [(0, SPLIT), (SPLIT, PAIRS)]
    assert LOOPED == LAST and LOOPED % 2 == 0 and QCOLS * QUARTERS == BUCKETS

    x_view = x.rearrange("(g r) (i k) -> i r g k", r=ROWS, i=QUARTERS)

    def emb_rows(i, start, pairs):
        a = i * QCOLS + start
        return emb[bass.ds(a, pairs * PAIR), :].rearrange("(q r t) d -> r q (t d)", r=ROWS, t=2)

    ctx = ExitStack()
    with ctx:
        def sb(name, shape, dt=fp32):
            return ctx.enter_context(nc.sbuf_tensor(name, shape, dt))

        def ps(name):
            return ctx.enter_context(nc.psum_tensor(name, [P, 512], fp32))

        def sem(name):
            return ctx.enter_context(nc.semaphore(name))

        xt = [sb(f"x_tile{k}", [P, GROUPS, COLS]) for k in range(TILES)]
        tt = [sb(f"transposed{k}", [P, CHUNKS, TROWS]) for k in range(TILES)]
        et = [sb(f"emb{n}", [P, PAIRS, 2 * DIM]) for n in range(2)]
        e_last = sb("emb_last", [P, PAIRS, 2 * DIM])
        dump = sb("dump", [P, GROUPS, COLS], bf16)
        table_dump = sb("table_dump", [P, 1])
        partial = sb("partial_sums", [P, STEPS + 1, TILES * GROUPS])
        quarter_sums = sb("quarter_sums", [P, TILES * GROUPS])
        ident = sb("ident", [P, P])
        fold = sb("fold", [P, ROWS])
        zeros = sb("zeros", [P, TROWS], bf16)
        acc_sb = [sb(f"acc_sb{h}", [P, TROWS]) for h in range(2)]
        rowsum = sb("rowsum", [P, TILES * 2])
        inverse = sb("inverse", [P, TILES * 2])
        positive = sb("positive", [P, TILES * 2], u32)
        scaled = sb("scaled", [P, 4, 2, DIM])
        result = sb("result", [P, 4, 2, DIM])

        acc = [ps(f"acc{h}") for h in range(2)]
        sum_ps = ps("sum_ps")
        flip = [ps(f"flip{h}") for h in range(2)]

        x_landed = [[sem(f"x_landed{q}_{k}") for k in range(TILES)] for q in range(2)]
        part_landed = [[sem(f"part_landed{q}_{m}") for m in range(2)] for q in range(2)]
        e_landed = [sem(f"e_landed{n}") for n in range(2)]
        e_last_landed = sem("e_last_landed")
        tile_transposed = sem("tile_transposed")
        tile_summed = sem("tile_summed")
        half_multiplied = [sem(f"half_multiplied{h}") for h in range(2)]
        zeros_ready = sem("zeros_ready")
        pads_ready = sem("pads_ready")
        pad_cleared = sem("pad_cleared")
        ident_zeroed = sem("ident_zeroed")
        ident_ready = sem("ident_ready")
        fold_ready = sem("fold_ready")
        quarters_ready = sem("quarters_ready")
        sums_folded = sem("sums_folded")
        scale_ready = sem("scale_ready")
        sums_copied = sem("sums_copied")
        part_summed = sem("part_summed")
        acc_copied = sem("acc_copied")
        flipped = sem("flipped")
        result_zeroed = sem("result_zeroed")
        scaled_ready = sem("scaled_ready")
        result_ready = sem("result_ready")
        stored = sem("stored")

        block = ctx.enter_context(nc.Block())

        LOWER, UPPER = (1, 0), (2, 3)

        def tile_landed(eng, k, done):
            eng.wait_ge(x_landed[0][k], done)
            eng.wait_ge(x_landed[1][k], done)

        def part_in(eng, m):
            eng.wait_ge(part_landed[0][m], 64)
            eng.wait_ge(part_landed[1][m], 64)

        def held(eng, value):
            return value if isinstance(value, int) else eng.snap(value)

        def load_x(eng, quarters, k, start, cols=COLS):
            for i in quarters:
                eng.dma_start(xt[k][ROWS * i:ROWS * (i + 1), :, 0:cols],
                              x_view[i, :, GROUPS * k:GROUPS * (k + 1), bass.ds(start, cols)]
                              ).then_inc(x_landed[quarters is UPPER][k], 16)

        def part_cols(m):
            q0, q1 = PARTS[m]
            return q0 * PAIR, min(q1 * PAIR, LAST_COLS)

        def load_part(eng, quarters, m):
            c0, c1 = part_cols(m)
            for k in (2, 3):
                for i in quarters:
                    eng.dma_start(xt[k][ROWS * i:ROWS * (i + 1), :, c0:c1],
                                  x_view[i, :, GROUPS * k:GROUPS * (k + 1), LAST * COLS + c0:LAST * COLS + c1]
                                  ).then_inc(part_landed[quarters is UPPER][m], 16)

        def load_e(eng, n, start):
            for i in reversed(range(QUARTERS)):
                eng.dma_start(et[n][ROWS * i:ROWS * (i + 1), :, :],
                              emb_rows(i, start, PAIRS)).then_inc(e_landed[n], 16)

        def load_e_last(eng):
            eng.wait_ge(pads_ready, 1)
            for i in range(QUARTERS):
                p = ROWS * i
                start = LAST * COLS
                eng.dma_start(e_last[p:p + ROWS, 0:LAST_FULL, :],
                              emb_rows(i, start, LAST_FULL)).then_inc(e_last_landed, 16)
                row = i * QCOLS + start + LAST_FULL * PAIR
                both = LAST_REST // 2
                eng.dma_start(e_last[p:p + both, LAST_FULL, :],
                              emb[row:row + 2 * both, :].rearrange("(r t) d -> r (t d)", t=2)
                              ).then_inc(e_last_landed, 16)
                if LAST_REST % 2:
                    eng.dma_start(e_last[p + both:p + both + 1, LAST_FULL, 0:DIM],
                                  emb[row + 2 * both:row + 2 * both + 1, :]).then_inc(e_last_landed, 16)
        def slot_free(eng, done):
            eng.wait_ge(tile_transposed, done)
            eng.wait_ge(tile_summed, done)

        def load_last_step(eng, quarters, between=None):
            for k in range(2):
                slot_free(eng, 4 * (LAST - 1) + k + 1)
                load_x(eng, quarters, k, LAST * COLS, LAST_COLS)
            if between:
                between(eng)
            slot_free(eng, 4 * LAST)
            for m in range(2):
                load_part(eng, quarters, m)

        E_LAST = 16 * QUARTERS * (2 + LAST_REST % 2)

        @block.sync
        def _(sp):
            load_x(sp, LOWER, 0, 0)
            load_e(sp, 0, 0)
            for k in range(1, TILES):
                load_x(sp, LOWER, k, 0)

            def next_step(s, n):
                start = held(sp, (s + 1) * COLS)
                e_free = held(sp, s + 1)
                for k in range(TILES):
                    slot_free(sp, held(sp, 4 * s + k + 1))
                    load_x(sp, LOWER, k, start)
                    if k == 1:
                        sp.wait_ge(half_multiplied[1], e_free)
                        load_e(sp, 1 - n, start)

            with sp.Fori(0, LOOPED // 2 - 1, 1) as two:
                for n in range(2):
                    next_step(two * 2 + n, n)
            next_step(LAST - 2, 0)
            load_last_step(sp, LOWER, load_e_last)
            out_view = out.rearrange("(h a u p) d -> p h u a d", h=2, a=2, u=2)
            for h in range(2):
                sp.wait_ge(result_ready, h + 1)
                for u in range(2):
                    sp.dma_start(out_view[:, h, u, :, :], result[:, 2 * h + u, :, :]).then_inc(stored, 16)
            sp.wait_ge(stored, 64)

        @block.scalar
        def _(act):
            def sum_columns(k, slot, c0, c1):
                for n in range(GROUPS):
                    last = nc.scalar.activation(dump[:, n, 0:c1 - c0], xt[k][:, n, c0:c1], ACT.Copy,
                                                accum_out=partial[:, bass.ds(slot, 1), GROUPS * k + n])
                last.then_inc(tile_summed, 1)

            act.wait_ge(zeros_ready, 1)
            nc.scalar.activation(table_dump[:], zeros[:, 0:1], ACT.Copy)
            with act.Fori(0, LOOPED, 1) as s:
                landed = held(act, 32 * (s + 1))
                for k in range(TILES):
                    done = held(act, 4 * s + k + 1)
                    tile_landed(act, k, landed)
                    sum_columns(k, s, 0, COLS)
                    act.wait_ge(tile_summed, done)
            for k in range(2):
                tile_landed(act, k, 32 * STEPS)
                act.wait_ge(tile_summed, 4 * LAST + k)
                sum_columns(k, LAST, 0, LAST_COLS)
            for n, (m, k) in enumerate(((0, 2), (0, 3), (1, 2))):
                part_in(act, m)
                act.wait_ge(tile_summed, 4 * LAST + 2 + n)
                sum_columns(k, LAST + m, *part_cols(m))

        @block.gpsimd
        def _(pool):
            for k in range(TILES):
                load_x(pool, UPPER, k, 0)
            nc.gpsimd.memset(zeros[:], 0.0).then_inc(zeros_ready, 1)
            nc.gpsimd.memset(result[:], 0.0).then_inc(result_zeroed, 1)
            nc.gpsimd.memset(e_last[:, LAST_FULL, :], 0.0).then_inc(pads_ready, 1)
            nc.gpsimd.memset(ident[:], 0.0).then_inc(ident_zeroed, 1)
            pool.wait_ge(ident_zeroed, 1)
            nc.gpsimd.affine_select(out=ident[:], in_=ident[:], compare_op=ALU.not_equal, fill=1.0, base=0,
                                    pattern=[[-1, P]], channel_multiplier=1).then_inc(ident_ready, 1)
            with pool.Fori(0, LOOPED - 1, 1) as s:
                start = held(pool, (s + 1) * COLS)
                for k in range(TILES):
                    slot_free(pool, held(pool, 4 * s + k + 1))
                    load_x(pool, UPPER, k, start)
            load_last_step(pool, UPPER)

        @block.vector
        def _(dve):
            def transpose_tile(k):
                nc.vector.transpose(
                    tt[k][:].rearrange("p j (n c) -> p n j c", c=ROWS),
                    xt[k][:].rearrange("p n (q r t) -> p (n q) t r", t=2, r=ROWS)).then_inc(tile_transposed, 1)

            def clear_pad(k):
                nc.vector.memset(xt[k][:, :, LAST_COLS:COLS], 0.0).then_inc(pad_cleared, 1)

            dve.wait_ge(ident_ready, 1)
            nc.vector.tensor_reduce(fold[:], ident[:].rearrange("p (i r) -> p r i", r=ROWS),
                                    AX.X, ALU.add).then_inc(fold_ready, 1)
            with dve.Fori(0, LOOPED, 1) as s:
                landed = held(dve, 32 * (s + 1))
                free = held(dve, s + 1)
                for k in range(TILES):
                    tile_landed(dve, k, landed)
                    if k % 2 == 0:
                        dve.wait_ge(half_multiplied[k // 2], free)
                    transpose_tile(k)
            for k in range(2):
                tile_landed(dve, k, 32 * STEPS)
                clear_pad(k)
                if k == 0:
                    dve.wait_ge(half_multiplied[0], STEPS)
                dve.wait_ge(pad_cleared, k + 1)
                transpose_tile(k)

            def transpose_part(m):
                q0, q1 = PARTS[m]
                part_in(dve, m)
                if m == 0:
                    clear_pad(2)
                    clear_pad(3)
                    dve.wait_ge(half_multiplied[1], STEPS)
                    dve.wait_ge(pad_cleared, 4)
                for k in (2, 3):
                    for t in range(2):
                        last = nc.vector.transpose(
                            tt[k][:, 2 * q0 + t:2 * q1:2, :].rearrange("p q (n c) -> p n q c", c=ROWS),
                            xt[k][:, :, q0 * PAIR:q1 * PAIR].rearrange("p n (q r t) -> p t n q r",
                                                                       t=2, r=ROWS)[:, t])
                    last.then_inc(tile_transposed, 1)

            def sum_steps(h):
                g = slice(16 * h, 16 * h + 16)
                nc.vector.tensor_reduce(quarter_sums[:, g], partial[:, 0:STEPS + h, g].rearrange("p s g -> p g s"),
                                        AX.X, ALU.add).then_inc(quarters_ready, 1)

            def copy_acc(h):
                dve.wait_ge(half_multiplied[h], STEPS + 1)
                nc.vector.tensor_copy(acc_sb[h][:], acc[h][:, 0:TROWS]).then_inc(acc_copied, 1)

            def per_block(t, h):
                v = t[:, 4 * h:4 * h + 4].rearrange("p (a u) -> p u a", a=2)
                return v.unsqueeze(3).broadcast_to((P, 2, 2, DIM))

            def scales(h):
                b = slice(4 * h, 4 * h + 4)
                dve.wait_ge(sums_folded, h + 1)
                nc.vector.tensor_copy(rowsum[:, b], sum_ps[:, b]).then_inc(sums_copied, 1)
                dve.wait_ge(sums_copied, h + 1)
                nc.vector.tensor_scalar(positive[:, b], rowsum[:, b], 0.0, None, ALU.is_gt).then_inc(scale_ready, 1)
                nc.vector.reciprocal(inverse[:, b], rowsum[:, b]).then_inc(scale_ready, 1)

            def finish(h):
                blocks = slice(2 * h, 2 * h + 2)
                dve.wait_ge(scale_ready, 2 * h + 2)
                dve.wait_ge(flipped, h + 1)
                nc.vector.tensor_tensor(
                    scaled[:, blocks, :, :],
                    flip[h][:, 0:2 * P].rearrange("p (u a d) -> p u a d", u=2, a=2),
                    per_block(inverse, h), ALU.mult).then_inc(scaled_ready, 1)
                dve.wait_ge(scaled_ready, h + 1)
                if h == 0:
                    dve.wait_ge(result_zeroed, 1)
                nc.vector.copy_predicated(result[:, blocks, :, :], per_block(positive, h),
                                          scaled[:, blocks, :, :]).then_inc(result_ready, 1)

            transpose_part(0)
            copy_acc(0)
            dve.wait_ge(tile_summed, 4 * LAST + 2)
            sum_steps(0)
            transpose_part(1)
            c0, c1 = part_cols(1)
            nc.vector.tensor_reduce(partial[:, STEPS, 3 * GROUPS:4 * GROUPS], xt[3][:, :, c0:c1],
                                    AX.X, ALU.add).then_inc(part_summed, 1)
            scales(0)
            finish(0)
            dve.wait_ge(part_summed, 1)
            dve.wait_ge(tile_summed, 4 * LAST + 5)
            sum_steps(1)
            copy_acc(1)
            scales(1)
            finish(1)

        @block.tensor
        def _(pe):
            def multiply(h, e, chunks=range(CHUNKS), final=False):
                for j in chunks:
                    for a in range(2):
                        mm = nc.tensor.matmul(acc[h][64 * a:64 * a + 64, 0:TROWS],
                                              e[:, j // 2, DIM * (j % 2):DIM * (j % 2 + 1)],
                                              tt[2 * h + a][:, j, :],
                                              start=False, stop=final and j == CHUNKS - 1)
                return mm

            pe.wait_ge(zeros_ready, 1)
            for h in range(2):
                for a in range(2):
                    mm = nc.tensor.matmul(acc[h][64 * a:64 * a + 64, 0:TROWS], zeros[:, 0:DIM], zeros[:],
                                          start=True, stop=False)
                mm.then_inc(half_multiplied[h], 1)
            with pe.Fori(0, LOOPED // 2, 1) as two:
                for n in range(2):
                    pe.wait_ge(e_landed[n], 64 * two + 64)
                    for h in range(2):
                        pe.wait_ge(tile_transposed, 8 * two + (4 * n + 2 * h + 2))
                        multiply(h, et[n]).then_inc(half_multiplied[h], 1)

            def fold_sums(h):
                pe.wait_ge(quarters_ready, h + 1)
                by_part = quarter_sums[:].rearrange("p (b w) -> p w b", w=4)
                for w in range(4):
                    mm = nc.tensor.matmul(sum_ps[ROWS * w:ROWS * (w + 1), 4 * h:4 * h + 4], fold[:],
                                          by_part[:, w, 4 * h:4 * h + 4], start=True, stop=True)
                mm.then_inc(sums_folded, 1)

            def flip_half(h):
                pe.wait_ge(acc_copied, h + 1)
                for u in range(2):
                    mm = nc.tensor.transpose(flip[h][:, P * u:P * (u + 1)],
                                             acc_sb[h][:, P * u:P * (u + 1)], ident[:])
                mm.then_inc(flipped, 1)

            pe.wait_ge(e_last_landed, E_LAST)
            pe.wait_ge(tile_transposed, 4 * LAST + 2)
            multiply(0, e_last, final=True).then_inc(half_multiplied[0], 1)
            pe.wait_ge(tile_transposed, 4 * LAST + 4)
            multiply(1, e_last, range(0, 2 * SPLIT))
            pe.wait_ge(fold_ready, 1)
            fold_sums(0)
            flip_half(0)
            pe.wait_ge(tile_transposed, 4 * LAST + 6)
            multiply(1, e_last, range(2 * SPLIT, CHUNKS), final=True).then_inc(half_multiplied[1], 1)
            fold_sums(1)
            flip_half(1)


_INS = ["r_inputs", "L0_rec_embeddings"]
_OUTS = [((1024, 64), "float32")]


def kernel(**inputs):
    import numpy as _np
    import concourse.bacc as _bacc
    from concourse import mybir as _mybir
    from concourse.bass_utils import run_bass_kernel_spmd as _run

    nc = _bacc.Bacc("TRN2", target_bir_lowering=False, num_devices=1)
    arrays, args = {}, []
    for name in _INS:
        a = _np.ascontiguousarray(inputs[name])
        arrays[f"in_{name}_dram"] = a
        args.append(nc.dram_tensor(f"in_{name}_dram", a.shape, _mybir.dt.from_np(a.dtype), kind="ExternalInput").ap())
    for i, (shape, dtype) in enumerate(_OUTS):
        dt = _mybir.dt.from_np(_np.dtype(dtype))
        args.append(nc.dram_tensor(f"out_{i}_dram", shape, dt, kind="ExternalOutput").ap())
    rec_kernel(nc, *args)
    r = _run(nc, [arrays], core_ids=[0])
    got = tuple(r.results[0][f"out_{i}_dram"] for i in range(len(_OUTS)))
    return got[0]
```

```python
import concourse.bass as bass
from concourse import mybir
from contextlib import ExitStack



def rec_kernel(nc: bass.Bass, x: bass.AP, emb: bass.AP, out: bass.AP):
    fp32 = mybir.dt.float32
    bf16 = mybir.dt.bfloat16
    u32 = mybir.dt.uint32
    ALU = mybir.AluOpType
    ACT = mybir.ActivationFunctionType
    AX = mybir.AxisListType

    BATCH, BUCKETS = x.shape
    DIM = emb.shape[1]
    P = 128
    ROWS = 32
    QUARTERS = P // ROWS
    QCOLS = BUCKETS // QUARTERS
    PAIR = 2 * ROWS
    PAIRS = 7
    CHUNKS = 2 * PAIRS
    COLS = PAIRS * PAIR
    STEPS = -(-QCOLS // COLS)
    LAST = STEPS - 1
    LAST_COLS = QCOLS - LAST * COLS
    LAST_FULL = LAST_COLS // PAIR
    LAST_REST = LAST_COLS % PAIR
    TILES = 4
    GROUPS = BATCH // ROWS // TILES
    TROWS = GROUPS * ROWS
    ALONE = 4
    BLOCKS = BATCH // P
    LOOPED = 6
    PARTS = [(4, 7), (0, 2), (2, 4)]
    SLOTS = STEPS + 1
    assert LOOPED == LAST and LOOPED % 2 == 0 and QCOLS * QUARTERS == BUCKETS

    x_view = x.rearrange("(g r) (i k) -> i r g k", r=ROWS, i=QUARTERS)

    def emb_rows(i, start, pairs):
        a = i * QCOLS + start
        return emb[bass.ds(a, pairs * PAIR), :].rearrange("(q r t) d -> r q (t d)", r=ROWS, t=2)

    ctx = ExitStack()
    with ctx:
        def sb(name, shape, dt=fp32):
            return ctx.enter_context(nc.sbuf_tensor(name, shape, dt))

        def ps(name):
            return ctx.enter_context(nc.psum_tensor(name, [P, 512], fp32))

        def sem(name):
            return ctx.enter_context(nc.semaphore(name))

        x_all = sb("x_all", [P, TILES * GROUPS, COLS])
        xt = [x_all[:, GROUPS * k:GROUPS * (k + 1), :] for k in range(TILES)]
        tt = [sb(f"transposed{k}", [P, CHUNKS, TROWS]) for k in range(TILES)]
        et = [sb(f"emb{n}", [P, PAIRS, 2 * DIM]) for n in range(2)]
        e_last = sb("emb_last", [P, PAIRS, 2 * DIM])
        dump = sb("dump", [P, GROUPS, COLS], bf16)
        folded = sb("folded", [P, 2, GROUPS, 2 * PAIR])
        table_dump = sb("table_dump", [P, 1])
        partial = sb("partial_sums", [P, SLOTS, TILES * GROUPS])
        quarter_sums = sb("quarter_sums", [P, TILES * GROUPS])
        ident = sb("ident", [P, P])
        fold = sb("fold", [P, ROWS])
        zeros = sb("zeros", [P, TROWS], bf16)
        acc_sb = [sb(f"acc_sb{h}", [P, TROWS]) for h in range(2)]
        inverse = sb("inverse", [P, BLOCKS])
        positive = sb("positive", [P, BLOCKS], u32)
        scaled = sb("scaled", [P, BLOCKS, DIM])
        result = sb("result", [P, BLOCKS, DIM])

        acc = [ps(f"acc{h}") for h in range(2)]
        sum_ps = ps("sum_ps")
        flip = [ps(f"flip{h}")[:, :].rearrange("p (b d) -> p b d", d=DIM)[:, 0:BLOCKS // 2] for h in range(2)]

        x_landed = [[sem(f"x_landed{q}_{k}") for k in range(TILES)] for q in range(2)]
        part_landed = [[sem(f"part_landed{h}_{m}") for m in range(len(PARTS))] for h in range(2)]
        e_landed = [sem(f"e_landed{n}") for n in range(2)]
        e_last_landed = sem("e_last_landed")
        tile_transposed = sem("tile_transposed")
        part_transposed = sem("part_transposed")
        tile_summed = sem("tile_summed")
        half_multiplied = [sem(f"half_multiplied{h}") for h in range(2)]
        zeros_ready = sem("zeros_ready")
        pads_ready = sem("pads_ready")
        pad_cleared = sem("pad_cleared")
        ident_zeroed = sem("ident_zeroed")
        ident_ready = sem("ident_ready")
        fold_ready = sem("fold_ready")
        quarters_ready = sem("quarters_ready")
        sums_folded = sem("sums_folded")
        scale_ready = sem("scale_ready")
        fold_step = sem("fold_step")
        part_summed = sem("part_summed")
        acc_copied = sem("acc_copied")
        flipped = sem("flipped")
        result_zeroed = sem("result_zeroed")
        scaled_ready = sem("scaled_ready")
        result_ready = sem("result_ready")
        stored = sem("stored")

        block = ctx.enter_context(nc.Block())

        LOWER, UPPER = (1, 0), (2, 3)

        def tile_landed(eng, k, done):
            eng.wait_ge(x_landed[0][k], done)
            eng.wait_ge(x_landed[1][k], done)

        def held(eng, value):
            return value if isinstance(value, int) else eng.snap(value)

        def load_x(eng, quarters, k, start, cols=COLS):
            for i in quarters:
                eng.dma_start(xt[k][ROWS * i:ROWS * (i + 1), :, 0:cols],
                              x_view[i, :, GROUPS * k:GROUPS * (k + 1), bass.ds(start, cols)]
                              ).then_inc(x_landed[quarters is UPPER][k], 16)

        def part_cols(m):
            q0, q1 = PARTS[m]
            return q0 * PAIR, min(q1 * PAIR, LAST_COLS)

        def load_part(eng, h, m):
            c0, c1 = part_cols(m)
            g = slice(2 * GROUPS * h, 2 * GROUPS * (h + 1))
            for i in (0, 2, 1, 3):
                eng.dma_start(x_all[ROWS * i:ROWS * (i + 1), g, c0:c1],
                              x_view[i, :, g, LAST * COLS + c0:LAST * COLS + c1]
                              ).then_inc(part_landed[h][m], 16)

        OTHERS = (part_cols(1)[0], part_cols(2)[1])
        NARROW = part_cols(1)[1]

        def load_e(eng, n, start):
            for i in reversed(range(QUARTERS)):
                eng.dma_start(et[n][ROWS * i:ROWS * (i + 1), :, :],
                              emb_rows(i, start, PAIRS)).then_inc(e_landed[n], 16)

        def load_e_last(eng):
            eng.wait_ge(pads_ready, 1)
            for i in range(QUARTERS):
                p = ROWS * i
                start = LAST * COLS
                eng.dma_start(e_last[p:p + ROWS, 0:LAST_FULL, :],
                              emb_rows(i, start, LAST_FULL)).then_inc(e_last_landed, 16)
                row = i * QCOLS + start + LAST_FULL * PAIR
                both = LAST_REST // 2
                eng.dma_start(e_last[p:p + both, LAST_FULL, :],
                              emb[row:row + 2 * both, :].rearrange("(r t) d -> r (t d)", t=2)
                              ).then_inc(e_last_landed, 16)
                if LAST_REST % 2:
                    eng.dma_start(e_last[p + both:p + both + 1, LAST_FULL, 0:DIM],
                                  emb[row + 2 * both:row + 2 * both + 1, :]).then_inc(e_last_landed, 16)

        def slot_free(eng, done):
            eng.wait_ge(tile_transposed, done)
            eng.wait_ge(tile_summed, done)

        def load_last_step(eng, h, parts):
            slot_free(eng, 4 * (LAST - 1) + 2 * h + 2)
            for m in parts:
                load_part(eng, h, m)

        E_LAST = 16 * QUARTERS * (2 + LAST_REST % 2)

        def store(eng, h):
            b = slice(BLOCKS // 2 * h, BLOCKS // 2 * (h + 1))
            eng.wait_ge(result_ready, h + 1)
            eng.dma_start(out.rearrange("(b p) d -> p b d", p=P)[:, b, :], result[:, b, :]).then_inc(stored, 16)

        @block.sync
        def _(sp):
            load_x(sp, LOWER, 0, 0)
            load_e(sp, 0, 0)
            for k in range(1, TILES):
                load_x(sp, LOWER, k, 0)
            load_e_last(sp)

            def next_step(s, n):
                start = held(sp, (s + 1) * COLS)
                e_free = held(sp, s + 1)
                for k in range(TILES):
                    slot_free(sp, held(sp, 4 * s + k + 1))
                    load_x(sp, LOWER, k, start)
                    if k == 1:
                        sp.wait_ge(half_multiplied[1], e_free)
                        load_e(sp, 1 - n, start)

            with sp.Fori(0, LOOPED // 2 - 1, 1) as two:
                for n in range(2):
                    next_step(two * 2 + n, n)
            next_step(LAST - 2, 0)
            load_last_step(sp, 0, (0, 1))
            load_last_step(sp, 1, (0, 1, 2))
            store(sp, 0)
            sp.wait_ge(stored, 32)

        @block.scalar
        def _(act):
            def sum_columns(k, slot, c0, c1):
                for n in range(GROUPS):
                    last = nc.scalar.activation(dump[:, n, 0:c1 - c0], xt[k][:, n, c0:c1], ACT.Copy,
                                                accum_out=partial[:, bass.ds(slot, 1), GROUPS * k + n])
                last.then_inc(tile_summed, 1)

            act.wait_ge(zeros_ready, 1)
            nc.scalar.activation(table_dump[:], zeros[:, 0:1], ACT.Copy)
            with act.Fori(0, LOOPED, 1) as s:
                landed = held(act, 32 * (s + 1))
                for k in range(TILES):
                    done = held(act, 4 * s + k + 1)
                    tile_landed(act, k, landed)
                    sum_columns(k, s, 0, COLS)
                    act.wait_ge(tile_summed, done)
            for h in range(2):
                act.wait_ge(part_landed[h][0], 64)
                for n, k in enumerate((2 * h, 2 * h + 1)):
                    sum_columns(k, LAST, *part_cols(0))
                    act.wait_ge(tile_summed, 4 * LAST + 3 * h + n + 1)
                act.wait_ge(part_landed[h][1], 64)
                act.wait_ge(part_landed[h][2], 64)
                sum_columns(2 * h, LAST + 1, *OTHERS)
                act.wait_ge(tile_summed, 4 * LAST + 3 * h + 3)
            for h in range(2):
                act.wait_ge(half_multiplied[h], STEPS + 1)
                nc.scalar.copy(acc_sb[h][:], acc[h][:, 0:TROWS]).then_inc(acc_copied, 1)
            store(act, 1)

        @block.gpsimd
        def _(pool):
            nc.gpsimd.memset(e_last[:, LAST_FULL, :], 0.0).then_inc(pads_ready, 1)
            for k in range(TILES):
                load_x(pool, UPPER, k, 0)
            nc.gpsimd.memset(zeros[:], 0.0).then_inc(zeros_ready, 1)
            nc.gpsimd.memset(result[:], 0.0).then_inc(result_zeroed, 1)
            nc.gpsimd.memset(ident[:], 0.0).then_inc(ident_zeroed, 1)
            pool.wait_ge(ident_zeroed, 1)
            nc.gpsimd.affine_select(out=ident[:], in_=ident[:], compare_op=ALU.not_equal, fill=1.0, base=0,
                                    pattern=[[-1, P]], channel_multiplier=1).then_inc(ident_ready, 1)
            with pool.Fori(0, LOOPED - 1, 1) as s:
                start = held(pool, (s + 1) * COLS)
                for k in range(TILES):
                    slot_free(pool, held(pool, 4 * s + k + 1))
                    load_x(pool, UPPER, k, start)
            load_last_step(pool, 0, (2,))
            for h in range(2):
                k = 2 * h + 1
                (a, _), (b, _) = part_cols(1), part_cols(2)
                pool.wait_ge(part_landed[h][1], 64)
                pool.wait_ge(part_landed[h][2], 64)
                nc.gpsimd.tensor_tensor(folded[:, h], xt[k][:, :, a:a + NARROW], xt[k][:, :, b:b + NARROW],
                                        ALU.add).then_inc(fold_step, 1)
                pool.wait_ge(fold_step, 2 * h + 1)
                nc.gpsimd.tensor_tensor(folded[:, h, :, 0:NARROW // 2], folded[:, h, :, 0:NARROW // 2],
                                        folded[:, h, :, NARROW // 2:NARROW], ALU.add).then_inc(fold_step, 1)

        @block.vector
        def _(dve):
            def transpose_tile(k):
                nc.vector.transpose(
                    tt[k][:].rearrange("p j (n c) -> p n j c", c=ROWS),
                    xt[k].rearrange("p n (q r t) -> p (n q) t r", t=2, r=ROWS)).then_inc(tile_transposed, 1)

            dve.wait_ge(ident_ready, 1)
            nc.vector.tensor_reduce(fold[:], ident[:].rearrange("p (i r) -> p r i", r=ROWS),
                                    AX.X, ALU.add).then_inc(fold_ready, 1)
            with dve.Fori(0, LOOPED, 1) as s:
                landed = held(dve, 32 * (s + 1))
                free = held(dve, s + 1)
                for k in range(TILES):
                    tile_landed(dve, k, landed)
                    if k % 2 == 0:
                        dve.wait_ge(half_multiplied[k // 2], free)
                    transpose_tile(k)

            def transpose_part(h, m):
                q0, q1 = PARTS[m]
                if m == 0:
                    slot_free(dve, 4 * (LAST - 1) + 2 * h + 2)
                    for k in (2 * h, 2 * h + 1):
                        nc.vector.memset(xt[k][:, :, LAST_COLS:COLS], 0.0).then_inc(pad_cleared, 1)
                    dve.wait_ge(half_multiplied[h], STEPS)
                    dve.wait_ge(pad_cleared, 2 * h + 2)
                dve.wait_ge(part_landed[h][m], 64)
                for t in range(2):
                    for k in (2 * h, 2 * h + 1):
                        last = nc.vector.transpose(
                            tt[k][:, 2 * q0 + t:2 * q1:2, :].rearrange("p q (n c) -> p n q c", c=ROWS),
                            xt[k][:, :, q0 * PAIR:q1 * PAIR].rearrange("p n (q r t) -> p t n q r",
                                                                       t=2, r=ROWS)[:, t])
                    last.then_inc(part_transposed, 1)

            def sum_folded(h):
                k = 2 * h + 1
                dve.wait_ge(fold_step, 2 * h + 2)
                nc.vector.tensor_reduce(partial[:, LAST + 1, GROUPS * k:GROUPS * (k + 1)],
                                        folded[:, h, :, 0:NARROW // 2], AX.X, ALU.add).then_inc(part_summed, 1)

            def over_block(t, b):
                return t[:, b].unsqueeze(2).broadcast_to((P, BLOCKS // 2, DIM))

            for h in range(2):
                for m in range(len(PARTS)):
                    transpose_part(h, m)
                sum_folded(h)
            dve.wait_ge(tile_summed, 4 * LAST + 3 * 2)
            dve.wait_ge(part_summed, 2)
            nc.vector.tensor_reduce(quarter_sums[:], partial[:].rearrange("p s g -> p g s"),
                                    AX.X, ALU.add).then_inc(quarters_ready, 1)
            dve.wait_ge(sums_folded, 1)
            nc.vector.reciprocal(inverse[:], sum_ps[:, 0:BLOCKS]).then_inc(scale_ready, 1)
            nc.vector.tensor_scalar(positive[:], sum_ps[:, 0:BLOCKS], 0.0, None, ALU.is_gt).then_inc(scale_ready, 1)
            dve.wait_ge(scale_ready, 2)
            halves = [slice(0, BLOCKS // 2), slice(BLOCKS // 2, BLOCKS)]
            for h, b in enumerate(halves):
                dve.wait_ge(flipped, h + 1)
                nc.vector.tensor_tensor(scaled[:, b, :], flip[h], over_block(inverse, b),
                                        ALU.mult).then_inc(scaled_ready, 1)
            dve.wait_ge(result_zeroed, 1)
            for h, b in enumerate(halves):
                dve.wait_ge(scaled_ready, h + 1)
                nc.vector.copy_predicated(result[:, b, :], over_block(positive, b),
                                          scaled[:, b, :]).then_inc(result_ready, 1)

        @block.tensor
        def _(pe):
            def multiply(h, e, chunks=range(CHUNKS), tiles=(0, 1), final=False):
                for j in chunks:
                    for a in tiles:
                        mm = nc.tensor.matmul(acc[h][64 * a:64 * a + 64, 0:TROWS],
                                              e[:, j // 2, DIM * (j % 2):DIM * (j % 2 + 1)],
                                              tt[2 * h + a][:, j, :],
                                              start=False, stop=final and j == chunks[-1])
                return mm

            pe.wait_ge(zeros_ready, 1)
            for h in range(2):
                for a in range(2):
                    mm = nc.tensor.matmul(acc[h][64 * a:64 * a + 64, 0:TROWS], zeros[:, 0:DIM], zeros[:],
                                          start=True, stop=False)
                mm.then_inc(half_multiplied[h], 1)
            with pe.Fori(0, LOOPED // 2, 1) as two:
                for n in range(2):
                    pe.wait_ge(e_landed[n], 64 * two + 64)
                    for h in range(2):
                        pe.wait_ge(tile_transposed, 8 * two + (4 * n + 2 * h + 1))
                        multiply(h, et[n], range(ALONE), (0,))
                        pe.wait_ge(tile_transposed, 8 * two + (4 * n + 2 * h + 2))
                        multiply(h, et[n], range(ALONE, CHUNKS))
                        multiply(h, et[n], range(ALONE), (1,)).then_inc(half_multiplied[h], 1)

            def flip_half(h):
                pe.wait_ge(acc_copied, h + 1)
                for u in range(2):
                    mm = nc.tensor.transpose(flip[h][:, u::2, :],
                                             acc_sb[h][:, P * u:P * (u + 1)], ident[:])
                return mm

            pe.wait_ge(e_last_landed, E_LAST)
            pe.wait_ge(fold_ready, 1)
            for h in range(2):
                for m, (q0, q1) in enumerate(PARTS):
                    for t in range(2):
                        pe.wait_ge(part_transposed, 2 * (len(PARTS) * h + m) + t + 1)
                        last = multiply(h, e_last, range(2 * q0 + t, 2 * q1, 2),
                                        final=m == len(PARTS) - 1 and t == 1)
                last.then_inc(half_multiplied[h], 1)
            flip_half(0).then_inc(flipped, 1)
            pe.wait_ge(quarters_ready, 1)
            by_part = quarter_sums[:].rearrange("p (b w) -> p w b", w=4)
            for w in range(4):
                mm = nc.tensor.matmul(sum_ps[ROWS * w:ROWS * (w + 1), 0:BLOCKS], fold[:], by_part[:, w, :],
                                      start=True, stop=True)
            mm.then_inc(sums_folded, 1)
            flip_half(1).then_inc(flipped, 1)


_INS = ["r_inputs", "L0_rec_embeddings"]
_OUTS = [((1024, 64), "float32")]


def kernel(**inputs):
    import numpy as _np
    import concourse.bacc as _bacc
    from concourse import mybir as _mybir
    from concourse.bass_utils import run_bass_kernel_spmd as _run

    nc = _bacc.Bacc("TRN2", target_bir_lowering=False, num_devices=1)
    arrays, args = {}, []
    for name in _INS:
        a = _np.ascontiguousarray(inputs[name])
        arrays[f"in_{name}_dram"] = a
        args.append(nc.dram_tensor(f"in_{name}_dram", a.shape, _mybir.dt.from_np(a.dtype), kind="ExternalInput").ap())
    for i, (shape, dtype) in enumerate(_OUTS):
        dt = _mybir.dt.from_np(_np.dtype(dtype))
        args.append(nc.dram_tensor(f"out_{i}_dram", shape, dt, kind="ExternalOutput").ap())
    rec_kernel(nc, *args)
    r = _run(nc, [arrays], core_ids=[0])
    got = tuple(r.results[0][f"out_{i}_dram"] for i in range(len(_OUTS)))
    return got[0]
```
